# Optimizing a Trainium2 kernel written in Bass

```python
import numpy as np
import jax
import jax.numpy as jnp

def _softmax(x, axis=-1):
    return jax.nn.softmax(x, axis=axis)

def _gelu(x):
    return jax.nn.gelu(x, approximate=True)

def _silu(x):
    return jax.nn.silu(x)

def _sigmoid(x):
    return jax.nn.sigmoid(x)

def _layernorm(x, axis=-1, eps=1e-05):
    m = jnp.mean(x, axis=axis, keepdims=True)
    v = jnp.var(x, axis=axis, keepdims=True)
    return (x - m) / jnp.sqrt(v + eps)

def _scatter_add(tgt, idx, src, axis=0):
    return tgt.at[idx].add(src)

def _segment_sum(src, seg, n):
    return jax.ops.segment_sum(src, seg, n)
kernel_name = 'mk_rec_standalone_d1_rec_r8_7617a6'

def setup_inputs(seed: int=0):
    np.random.seed(seed)
    _w = jnp.asarray

    def _rec_inputs():
        import jax
        import jax.numpy as jnp
        _rk = jax.random.key(seed)
        r_inputs = jax.random.uniform(jax.random.fold_in(_rk, 1), (512, 12500), jnp.float32, 0.0, 1)
        return r_inputs
    r_inputs = _rec_inputs()

    def _L0_rec_setup():
        import jax, jax.numpy as jnp
        import numpy as np
        BATCH = 256
        BUCKETS = 12500
        DIM = 64
        key = jax.random.key(seed)
        k1, k2 = jax.random.split(key)
        inputs = jax.random.uniform(k1, (BATCH, BUCKETS), dtype=jnp.float32)
        embeddings = jax.random.normal(k2, (BUCKETS, DIM), dtype=jnp.float32)
        return {'inputs': inputs, 'embeddings': embeddings}
    _L0_rec_all = _L0_rec_setup()
    _L0_rec_in = {k: v for k, v in _L0_rec_all.items() if k in ('embeddings',)}
    del _L0_rec_all
    return {'r_inputs': r_inputs, 'L0_rec_embeddings': _L0_rec_in['embeddings']}

def reference(r_inputs, L0_rec_embeddings):
    import jax
    import jax.numpy as jnp

    def _L0_rec_ref(inputs, embeddings):
        import jax, jax.numpy as jnp
        import numpy as np
        BATCH = 256
        BUCKETS = 12500
        DIM = 64
        out = jnp.matmul(inputs, embeddings)
        s = jnp.sum(inputs, axis=-1, keepdims=True)
        out = jnp.where(s > 0, out / s, jnp.zeros_like(out))
        return out
    y = _L0_rec_ref(r_inputs, L0_rec_embeddings)
    return y

_drawn_inputs = setup_inputs


def setup_inputs(seed=0):
    import zlib

    import numpy as np

    out = dict(_drawn_inputs(seed))
    spreads = {}
    factors = {}
    for name, (base, spread) in spreads.items():
        noise = np.random.default_rng([zlib.crc32(name.encode()), seed]).standard_normal(out[name].shape)
        drawn = base * np.exp(spread * noise) if base else spread * noise
        out[name] = jnp.asarray(drawn.astype(out[name].dtype))
    for name, factor in factors.items():
        out[name] = (out[name] * factor).astype(out[name].dtype)
    return out
```

```python
from contextlib import ExitStack

import concourse.bass as bass
from concourse import mybir

ALU = mybir.AluOpType
AX = mybir.AxisListType
F32 = mybir.dt.float32
U32 = mybir.dt.uint32

P = 128
ROWS = 512
BUCKETS = 12500
DIM = 64
HALF = ROWS // 2
WIDTH = ROWS + DIM

CHUNKS = 4
SLOTS = 4
BLOCK = CHUNKS * P
BLOCKS = BUCKETS // BLOCK
ROUNDS = BLOCKS // SLOTS
assert BLOCKS == ROUNDS * SLOTS
HEAD = BUCKETS - BLOCKS * BLOCK
HEAD_CHUNKS = [HEAD % P, P]
assert sum(HEAD_CHUNKS) == HEAD
LAST = BLOCKS - 1


def weighted_mean_kernel(nc, packed, out):
    def block_source(first_bucket):
        return packed[bass.ds(first_bucket, BLOCK), :].rearrange("(p c) f -> p c f", c=CHUNKS)

    with ExitStack() as ctx:
        def sb(name, shape, dt=F32):
            return ctx.enter_context(nc.sbuf_tensor(name, shape, dt))

        def psum(name, shape):
            return ctx.enter_context(nc.psum_tensor(name, shape, F32))

        def sem(name):
            return ctx.enter_context(nc.semaphore(name))

        ring = sb("ring", [P, SLOTS, CHUNKS, WIDTH])
        head = sb("head", [P, len(HEAD_CHUNKS), WIDTH])
        ones = sb("ones", [P, DIM])
        lane_sum = sb("lane_sum", [P, ROWS])
        inverse = sb("inverse", [P, HALF])
        positive = sb("positive", [P, HALF], U32)
        quotient = sb("quotient", [P, HALF])
        result = sb("result", [P, HALF])

        products = psum("products", [P, HALF])
        sums = psum("sums", [P, HALF])
        lane_acc = psum("lane_acc", [P, CHUNKS, ROWS])

        head_loaded = [sem(f"head_loaded{i}") for i in range(len(HEAD_CHUNKS))]
        slot_loaded = [sem(f"slot_loaded{s}") for s in range(SLOTS)]
        last_loaded = [sem(f"last_loaded{c}") for c in range(CHUNKS)]
        slot_used = [sem(f"slot_used{s}") for s in range(SLOTS)]
        block_added = sem("block_added")
        constants_set = sem("constants_set")
        lanes_cleared = sem("lanes_cleared")
        lanes_summed = sem("lanes_summed")
        sums_done = sem("sums_done")
        products_done = sem("products_done")
        finish_step = sem("finish_step")
        out_stored = sem("out_stored")

        block = ctx.enter_context(nc.Block())

        @block.sync
        def _(sp):
            at = 0
            for i, n in enumerate(HEAD_CHUNKS):
                sp.dma_start(head[0:n, i, :], packed[at:at + n, :]).then_inc(head_loaded[i], 16)
                at += n
            for s in range(SLOTS):
                sp.dma_start(ring[:, s], block_source(HEAD + s * BLOCK)).then_inc(slot_loaded[s], 16)
            with sp.Fori(1, ROUNDS - 1) as r:
                for s in range(SLOTS):
                    first_bucket = sp.snap((r * SLOTS + s) * BLOCK + HEAD)
                    sp.wait_ge(slot_used[s], r * 2)
                    sp.dma_start(ring[:, s], block_source(first_bucket)).then_inc(slot_loaded[s], 16)
            for s in range(SLOTS):
                b = (ROUNDS - 1) * SLOTS + s
                sp.wait_ge(slot_used[s], (ROUNDS - 1) * 2)
                src = block_source(HEAD + b * BLOCK)
                if b < LAST:
                    sp.dma_start(ring[:, s], src).then_inc(slot_loaded[s], 16)
                else:
                    for c in range(CHUNKS):
                        sp.dma_start(ring[:, s, c], src[:, c]).then_inc(last_loaded[c], 16)
            sp.wait_ge(finish_step, 3)
            sp.dma_start(out[:, :], result[:, :]).then_inc(out_stored, 16)
            sp.wait_ge(out_stored, 16)

        @block.tensor
        def _(pe):
            def both_tiles(bank, stationary, rows, start=False, stop=False):
                for t in range(2):
                    mm = nc.tensor.matmul(bank[DIM * t:DIM * (t + 1), :], stationary,
                                          rows[:, HALF * t:HALF * (t + 1)], start=start, stop=stop)
                return mm

            def multiply(chunk, start=False, stop=False):
                return both_tiles(products, chunk[:, ROWS:WIDTH], chunk[:, 0:ROWS], start, stop)

            pe.wait_ge(constants_set, 2)
            for i, n in enumerate(HEAD_CHUNKS):
                pe.wait_ge(head_loaded[i], 16)
                multiply(head[0:n, i, :], start=(i == 0))
                both_tiles(sums, ones[0:n, :], head[0:n, i, 0:ROWS], start=(i == 0))
            with pe.Fori(0, ROUNDS - 1) as r:
                for s in range(SLOTS):
                    pe.wait_ge(slot_loaded[s], (r + 1) * 16)
                    for c in range(CHUNKS):
                        mm = multiply(ring[:, s, c, :])
                    mm.then_inc(slot_used[s], 1)
            for s in range(SLOTS - 1):
                pe.wait_ge(slot_loaded[s], ROUNDS * 16)
                for c in range(CHUNKS):
                    multiply(ring[:, s, c, :])
            for c in range(CHUNKS):
                chunk = ring[:, SLOTS - 1, c, :]
                if c == CHUNKS - 1:
                    pe.wait_ge(lanes_summed, 1)
                    both_tiles(sums, ones[:, :], lane_sum[:, :])
                pe.wait_ge(last_loaded[c], 16)
                last = c == CHUNKS - 1
                mm = both_tiles(sums, ones[:, :], chunk[:, 0:ROWS], stop=last)
                if last:
                    mm.then_inc(sums_done, 1)
                mm = multiply(chunk, stop=last)
                if last:
                    mm.then_inc(products_done, 1)

        @block.vector
        def _(dve):
            def add_block(s, adds):
                nc.vector.tensor_tensor(lane_acc[:, :, :], ring[:, s, :, 0:ROWS], lane_acc[:, :, :],
                                        ALU.add).then_inc(block_added, 1)
                dve.wait_ge(block_added, adds)
                dve.sem_inc(slot_used[s], 1)

            nc.vector.memset(lane_acc[:, :, :], 0.0).then_inc(lanes_cleared, 1)
            dve.wait_ge(lanes_cleared, 1)
            with dve.Fori(0, ROUNDS - 1) as r:
                for s in range(SLOTS):
                    dve.wait_ge(slot_loaded[s], (r + 1) * 16)
                    add_block(s, r * SLOTS + s + 1)
            for s in range(SLOTS - 1):
                dve.wait_ge(slot_loaded[s], ROUNDS * 16)
                add_block(s, (ROUNDS - 1) * SLOTS + s + 1)
            nc.vector.tensor_reduce(lane_sum[:, :], lane_acc[:, :, :].rearrange("p c r -> p r c"), AX.X,
                                    ALU.add).then_inc(lanes_summed, 1)
            dve.wait_ge(sums_done, 1)
            nc.vector.reciprocal(inverse[:, :], sums[:, :]).then_inc(finish_step, 1)
            nc.vector.tensor_scalar(positive[:, :], sums[:, :], 0.0, None, ALU.is_gt)
            dve.wait_ge(finish_step, 1)
            dve.wait_ge(products_done, 1)
            nc.vector.tensor_tensor(quotient[:, :], products[:, :], inverse[:, :], ALU.mult).then_inc(finish_step, 1)
            dve.wait_ge(finish_step, 2)
            dve.wait_ge(constants_set, 2)
            nc.vector.copy_predicated(result[:, :], positive[:, :], quotient[:, :]).then_inc(finish_step, 1)

        @block.gpsimd
        def _(pool):
            nc.gpsimd.memset(ones[:, :], 1.0).then_inc(constants_set, 1)
            nc.gpsimd.memset(result[:, :], 0.0).then_inc(constants_set, 1)


def kernel(r_inputs, L0_rec_embeddings):
    import numpy as np
    import concourse.bacc as bacc
    from concourse.bass_utils import run_bass_kernel_spmd

    packed = np.concatenate([np.asarray(r_inputs).T, np.asarray(L0_rec_embeddings)], axis=1)
    nc = bacc.Bacc("TRN2", target_bir_lowering=False, num_devices=1)
    packed_dram = nc.dram_tensor("packed_dram", packed.shape, F32, kind="ExternalInput").ap()
    out_dram = nc.dram_tensor("out_dram", (P, HALF), F32, kind="ExternalOutput").ap()
    weighted_mean_kernel(nc, packed_dram, out_dram)
    ran = run_bass_kernel_spmd(nc, [{"packed_dram": packed}], core_ids=[0])
    got = ran.results[0]["out_dram"].reshape(2, DIM, HALF)
    return np.ascontiguousarray(got.transpose(0, 2, 1)).reshape(ROWS, DIM)
```

```python
from contextlib import ExitStack

import concourse.bass as bass
from concourse import mybir

ALU = mybir.AluOpType
AX = mybir.AxisListType
F32 = mybir.dt.float32
U32 = mybir.dt.uint32

P = 128
ROWS = 512
BUCKETS = 12500
DIM = 64
WIDTH = ROWS + DIM
TILES = P // DIM
TILE_ROWS = ROWS // TILES
GROUPS = ROWS // P
TILE_GROUPS = GROUPS // TILES

CHUNKS = 4
SLOTS = 4
BLOCK = CHUNKS * P
BLOCKS = BUCKETS // BLOCK
HEAD = BUCKETS - BLOCKS * BLOCK
HEAD_CHUNKS = [HEAD - P, P]
TAIL_BLOCKS = 2
RING_BLOCKS = BLOCKS - TAIL_BLOCKS
SPLIT = RING_BLOCKS - 1
ROUNDS = RING_BLOCKS // SLOTS
TAIL = TAIL_BLOCKS * CHUNKS
assert 0 < HEAD_CHUNKS[0] <= P and GROUPS == TILES * TILE_GROUPS and RING_BLOCKS > ROUNDS * SLOTS


def weighted_mean_kernel(nc, packed, out):
    def block_source(first_bucket):
        return packed[bass.ds(first_bucket, BLOCK), :].rearrange("(p c) f -> p c f", c=CHUNKS)

    with ExitStack() as ctx:
        def sb(name, shape, dt=F32):
            return ctx.enter_context(nc.sbuf_tensor(name, shape, dt))

        def psum(name, shape):
            return ctx.enter_context(nc.psum_tensor(name, shape, F32))

        def sem(name):
            return ctx.enter_context(nc.semaphore(name))

        ring = sb("ring", [P, SLOTS, CHUNKS, WIDTH])
        head = sb("head", [P, len(HEAD_CHUNKS), WIDTH])
        tail = sb("tail", [P, TAIL, WIDTH + 1])
        identity = sb("identity", [P, DIM])
        turned_in = sb("turned_in", [P, TILE_ROWS])
        lane_sum = sb("lane_sum", [P, ROWS])
        inverse = sb("inverse", [P, GROUPS])
        positive = sb("positive", [P, GROUPS], U32)
        quotient = sb("quotient", [P, GROUPS, DIM])
        result = sb("result", [P, GROUPS, DIM])

        lane_acc = psum("lane_acc", [P, CHUNKS, ROWS])
        products = psum("products", [P, ROWS])
        by_row = psum("by_row", [P, TILES, ROWS])
        groups = by_row[:, :, 0:TILE_GROUPS * (DIM + 1)].rearrange("p t (h w) -> p t h w", w=DIM + 1)
        row_sum = groups[:, :, :, DIM]

        head_loaded = [sem(f"head_loaded{i}") for i in range(len(HEAD_CHUNKS))]
        slot_loaded = [sem(f"slot_loaded{s}") for s in range(SLOTS)]
        split_loaded = [sem(f"split_loaded{c}") for c in range(CHUNKS)]
        tail_loaded = [sem(f"tail_loaded{c}") for c in range(TAIL)]
        slot_used = [sem(f"slot_used{s}") for s in range(SLOTS)]
        sums_cleared = sem("sums_cleared")
        head_added = sem("head_added")
        block_added = sem("block_added")
        lanes_summed = sem("lanes_summed")
        identity_step = sem("identity_step")
        ones_set = sem("ones_set")
        result_cleared = sem("result_cleared")
        products_done = sem("products_done")
        products_copied = sem("products_copied")
        rows_done = sem("rows_done")
        finish_step = sem("finish_step")
        out_stored = sem("out_stored")

        block = ctx.enter_context(nc.Block())

        @block.sync
        def _(sp):
            at = 0
            for i, n in enumerate(HEAD_CHUNKS):
                sp.dma_start(head[0:n, i, :], packed[at:at + n, :]).then_inc(head_loaded[i], 16)
                at += n
            for s in range(SLOTS):
                sp.dma_start(ring[:, s], block_source(HEAD + s * BLOCK)).then_inc(slot_loaded[s], 16)
            with sp.Fori(1, ROUNDS) as r:
                for s in range(SLOTS):
                    sp.wait_ge(slot_used[s], r * 2)
                    sp.dma_start(ring[:, s], block_source((r * SLOTS + s) * BLOCK + HEAD)).then_inc(slot_loaded[s], 16)
            for b in range(ROUNDS * SLOTS, RING_BLOCKS):
                s = b % SLOTS
                sp.wait_ge(slot_used[s], ROUNDS * 2)
                if b < SPLIT:
                    sp.dma_start(ring[:, s], block_source(HEAD + b * BLOCK)).then_inc(slot_loaded[s], 16)
                else:
                    for c in range(CHUNKS):
                        sp.dma_start(ring[:, s, c], block_source(HEAD + b * BLOCK)[:, c]).then_inc(split_loaded[c], 16)
            for c in range(TAIL):
                src = block_source(HEAD + (RING_BLOCKS + c // CHUNKS) * BLOCK)[:, c % CHUNKS]
                sp.dma_start(tail[:, c, 0:WIDTH], src).then_inc(tail_loaded[c], 16)
            sp.wait_ge(finish_step, 4)
            sp.dma_start(out[:, :, :], result[:, :, :]).then_inc(out_stored, 16)
            sp.wait_ge(out_stored, 16)

        @block.tensor
        def _(pe):
            def multiply(chunk, start=False, stop=False):
                for t in range(TILES):
                    mm = nc.tensor.matmul(products[DIM * t:DIM * (t + 1), 0:TILE_ROWS], chunk[:, ROWS:WIDTH],
                                          chunk[:, TILE_ROWS * t:TILE_ROWS * (t + 1)], start=start, stop=stop)
                return mm

            def add_by_row(held, streamed, first_column, stop=False):
                for g in range(GROUPS):
                    for t in range(TILES):
                        rows = P * g + DIM * t
                        mm = nc.tensor.matmul(
                            groups[DIM * t:DIM * (t + 1), g // TILE_GROUPS, g % TILE_GROUPS, first_column:],
                            held[:, rows:rows + DIM], streamed, start=False, stop=stop, skip_group_check=True)
                return mm

            for i, n in enumerate(HEAD_CHUNKS):
                pe.wait_ge(head_loaded[i], 16)
                multiply(head[0:n, i, :], start=(i == 0))
            with pe.Fori(0, ROUNDS) as r:
                for s in range(SLOTS):
                    pe.wait_ge(slot_loaded[s], (r + 1) * 16)
                    for c in range(CHUNKS):
                        mm = multiply(ring[:, s, c, :])
                    mm.then_inc(slot_used[s], 1)
            for b in range(ROUNDS * SLOTS, RING_BLOCKS):
                s = b % SLOTS
                if b < SPLIT:
                    pe.wait_ge(slot_loaded[s], (ROUNDS + 1) * 16)
                for c in range(CHUNKS):
                    if b == SPLIT:
                        pe.wait_ge(split_loaded[c], 16)
                    mm = multiply(ring[:, s, c, :], stop=(b == SPLIT and c == CHUNKS - 1))
            mm.then_inc(products_done, 1)

            pe.wait_ge(identity_step, 1 + TILES)
            pe.wait_ge(products_copied, 1)
            for g in range(GROUPS):
                t, h = g // TILE_GROUPS, g % TILE_GROUPS
                lanes = slice(DIM * t, DIM * (t + 1))
                nc.tensor.matmul(groups[:, t, h, 0:DIM], turned_in[lanes, P * h:P * (h + 1)], identity[lanes, :],
                                 is_transpose=True, start=(h == 0), stop=False, skip_group_check=True)
            pe.wait_ge(ones_set, 1)
            for c in range(TAIL):
                if c == TAIL - 1:
                    pe.wait_ge(lanes_summed, 1)
                    add_by_row(lane_sum, tail[:, 0, WIDTH:], DIM)
                pe.wait_ge(tail_loaded[c], 16)
                mm = add_by_row(tail[:, c, :], tail[:, c, ROWS:], 0, stop=(c == TAIL - 1))
            mm.then_inc(rows_done, 1)

        @block.vector
        def _(dve):
            def add_block(s, adds):
                nc.vector.tensor_tensor(lane_acc[:, :, :], ring[:, s, :, 0:ROWS], lane_acc[:, :, :],
                                        ALU.add).then_inc(block_added, 1)
                dve.wait_ge(block_added, adds)
                dve.sem_inc(slot_used[s], 1)

            nc.vector.memset(lane_acc[:, :, :], 0.0).then_inc(sums_cleared, 1)
            dve.wait_ge(sums_cleared, 1)
            for i, n in enumerate(HEAD_CHUNKS):
                dve.wait_ge(head_loaded[i], 16)
                nc.vector.tensor_tensor(lane_acc[0:n, i, :], head[0:n, i, 0:ROWS], lane_acc[0:n, i, :],
                                        ALU.add).then_inc(head_added, 1)
            dve.wait_ge(head_added, len(HEAD_CHUNKS))
            with dve.Fori(0, ROUNDS) as r:
                for s in range(SLOTS):
                    dve.wait_ge(slot_loaded[s], (r + 1) * 16)
                    add_block(s, r * SLOTS + s + 1)
            for b in range(ROUNDS * SLOTS, RING_BLOCKS):
                if b < SPLIT:
                    dve.wait_ge(slot_loaded[b % SLOTS], (ROUNDS + 1) * 16)
                else:
                    for c in range(CHUNKS):
                        dve.wait_ge(split_loaded[c], 16)
                add_block(b % SLOTS, b + 1)
            nc.vector.tensor_reduce(lane_sum[:, :], lane_acc[:, :, :].rearrange("p c r -> p r c"), AX.X,
                                    ALU.add).then_inc(lanes_summed, 1)

            dve.wait_ge(rows_done, 1)
            inverse_by_tile = inverse[:, :].rearrange("p (t h) -> p t h", t=TILES)
            positive_by_tile = positive[:, :].rearrange("p (t h) -> p t h", t=TILES)
            quotient_by_tile = quotient[:, :, :].rearrange("p (t h) d -> p t h d", t=TILES)
            nc.vector.reciprocal(inverse_by_tile, row_sum).then_inc(finish_step, 1)
            nc.vector.tensor_scalar(positive_by_tile, row_sum, 0.0, None, ALU.is_gt).then_inc(finish_step, 1)
            dve.wait_ge(finish_step, 1)
            nc.vector.tensor_tensor(quotient_by_tile, groups[:, :, :, 0:DIM],
                                    inverse_by_tile.unsqueeze(3).broadcast_to([P, TILES, TILE_GROUPS, DIM]), ALU.mult).then_inc(finish_step, 1)
            dve.wait_ge(finish_step, 3)
            dve.wait_ge(result_cleared, 1)
            nc.vector.copy_predicated(result[:, :, :], positive[:, :].unsqueeze(2).broadcast_to([P, GROUPS, DIM]),
                                      quotient[:, :, :]).then_inc(finish_step, 1)

        @block.scalar
        def _(act):
            act.wait_ge(products_done, 1)
            nc.scalar.copy(turned_in[:, :], products[:, 0:TILE_ROWS]).then_inc(products_copied, 1)

        @block.gpsimd
        def _(pool):
            nc.gpsimd.memset(identity[:, :], 0.0).then_inc(identity_step, 1)
            nc.gpsimd.memset(tail[:, :, WIDTH:], 1.0).then_inc(ones_set, 1)
            nc.gpsimd.memset(result[:, :, :], 0.0).then_inc(result_cleared, 1)
            for t in range(TILES):
                pool.wait_ge(identity_step, 1 + t)
                nc.gpsimd.affine_select(out=identity[:, :], in_=identity[:, :], compare_op=ALU.not_equal, fill=1.0,
                                        base=-DIM * t, pattern=[[-1, DIM]],
                                        channel_multiplier=1).then_inc(identity_step, 1)


def kernel(r_inputs, L0_rec_embeddings):
    import numpy as np
    import concourse.bacc as bacc
    from concourse.bass_utils import run_bass_kernel_spmd

    packed = np.concatenate([np.asarray(r_inputs).T, np.asarray(L0_rec_embeddings)], axis=1)
    nc = bacc.Bacc("TRN2", target_bir_lowering=False, num_devices=1)
    packed_dram = nc.dram_tensor("packed_dram", packed.shape, F32, kind="ExternalInput").ap()
    out_dram = nc.dram_tensor("out_dram", (P, GROUPS, DIM), F32, kind="ExternalOutput").ap()
    weighted_mean_kernel(nc, packed_dram, out_dram)
    ran = run_bass_kernel_spmd(nc, [{"packed_dram": packed}], core_ids=[0])
    return np.ascontiguousarray(ran.results[0]["out_dram"].transpose(1, 0, 2)).reshape(ROWS, DIM)
```

```python
from contextlib import ExitStack

import concourse.bass as bass
from concourse import mybir

ACT = mybir.ActivationFunctionType
ALU = mybir.AluOpType
AX = mybir.AxisListType
F32 = mybir.dt.float32
U32 = mybir.dt.uint32

P = 128
ROWS = 512
BUCKETS = 12500
DIM = 64
WIDTH = DIM + ROWS
TILES = P // DIM
TILE_ROWS = ROWS // TILES
GROUPS = ROWS // P
TILE_GROUPS = GROUPS // TILES

CHUNKS = 4
SLOTS = 4
BLOCK = CHUNKS * P
BLOCKS = BUCKETS // BLOCK
HEAD = BUCKETS - BLOCKS * BLOCK
HEAD_CHUNKS = [HEAD - P, P]
LANE_CHUNKS = CHUNKS - 1
READERS = 3

TAIL = 9
RING_CHUNKS = BLOCKS * CHUNKS - TAIL
RING_BLOCKS = RING_CHUNKS // CHUNKS
ROUNDS = (RING_BLOCKS - 1) // SLOTS
SINGLE = (RING_BLOCKS - 1) * CHUNKS
assert RING_BLOCKS == ROUNDS * SLOTS + 1
assert 0 < HEAD_CHUNKS[0] <= P and GROUPS == TILES * TILE_GROUPS and RING_CHUNKS % CHUNKS == LANE_CHUNKS


def weighted_mean_kernel(nc, packed, out):
    def chunk_source(index):
        return block_source(HEAD + index // CHUNKS * BLOCK)[:, index % CHUNKS]

    def block_source(first_bucket):
        return packed[bass.ds(first_bucket, BLOCK), :].rearrange("(p c) f -> p c f", c=CHUNKS)

    with ExitStack() as ctx:
        def sb(name, shape, dt=F32):
            return ctx.enter_context(nc.sbuf_tensor(name, shape, dt))

        def psum(name, shape):
            return ctx.enter_context(nc.psum_tensor(name, shape, F32))

        def sem(name):
            return ctx.enter_context(nc.semaphore(name))

        ring = sb("ring", [P, SLOTS, CHUNKS, WIDTH])
        head = sb("head", [P, len(HEAD_CHUNKS), WIDTH])
        tail = sb("tail", [P, TAIL, WIDTH + 1])
        identity = sb("identity", [P, DIM])
        turned_in = sb("turned_in", [P, TILE_ROWS])
        lane_sum = sb("lane_sum", [P, ROWS])
        pool_acc = sb("pool_acc", [P, ROWS])
        inverse = sb("inverse", [P, GROUPS])
        positive = sb("positive", [P, GROUPS], U32)
        quotient = sb("quotient", [P, GROUPS, DIM])
        result = sb("result", [P, GROUPS, DIM])

        lane_acc = psum("lane_acc", [P, LANE_CHUNKS, ROWS])
        lane_total = psum("lane_total", [P, ROWS])
        products = psum("products", [P, ROWS])
        by_row = psum("by_row", [P, TILES, ROWS])
        groups = by_row[:, :, 0:TILE_GROUPS * (DIM + 1)].rearrange("p t (h w) -> p t h w", w=DIM + 1)

        head_loaded = [sem(f"head_loaded{i}") for i in range(len(HEAD_CHUNKS))]
        slot_loaded = [sem(f"slot_loaded{s}") for s in range(SLOTS)]
        single_loaded = [sem(f"single_loaded{i}") for i in range(SINGLE, RING_CHUNKS)]
        tail_loaded = [sem(f"tail_loaded{c}") for c in range(TAIL)]
        last_half_loaded = sem("last_half_loaded")
        slot_used = [sem(f"slot_used{s}") for s in range(SLOTS)]
        sums_cleared = sem("sums_cleared")
        head_added = sem("head_added")
        block_added = sem("block_added")
        pool_cleared = sem("pool_cleared")
        pool_added = sem("pool_added")
        lanes_summed = sem("lanes_summed")
        identity_step = sem("identity_step")
        ones_set = sem("ones_set")
        result_cleared = sem("result_cleared")
        products_done = sem("products_done")
        products_copied = sem("products_copied")
        half_done = sem("half_done")
        inverted = sem("inverted")
        compared = sem("compared")
        first_half_divided = sem("first_half_divided")
        second_half_divided = sem("second_half_divided")
        selected = sem("selected")
        out_stored = sem("out_stored")

        block = ctx.enter_context(nc.Block())

        @block.sync
        def _(sp):
            at = 0
            for i, n in enumerate(HEAD_CHUNKS):
                sp.dma_start(head[0:n, i, :], packed[at:at + n, :]).then_inc(head_loaded[i], 16)
                at += n
            for s in range(SLOTS):
                sp.dma_start(ring[:, s], block_source(HEAD + s * BLOCK)).then_inc(slot_loaded[s], 16)
            with sp.Fori(1, ROUNDS) as r:
                for s in range(SLOTS):
                    sp.wait_ge(slot_used[s], r * READERS)
                    sp.dma_start(ring[:, s], block_source((r * SLOTS + s) * BLOCK + HEAD)).then_inc(slot_loaded[s], 16)
            for i in range(SINGLE, RING_CHUNKS):
                s, c = i // CHUNKS % SLOTS, i % CHUNKS
                if c == 0:
                    sp.wait_ge(slot_used[s], ROUNDS * READERS)
                sp.dma_start(ring[:, s, c], chunk_source(i)).then_inc(single_loaded[i - SINGLE], 16)
            for c in range(TAIL - 1):
                sp.dma_start(tail[:, c, 1:], chunk_source(RING_CHUNKS + c)).then_inc(tail_loaded[c], 16)
            src = chunk_source(RING_CHUNKS + TAIL - 1)
            cut = DIM + ROWS // 2
            sp.dma_start(tail[:, TAIL - 1, 1:1 + cut], src[:, 0:cut]).then_inc(tail_loaded[TAIL - 1], 16)
            sp.dma_start(tail[:, TAIL - 1, 1 + cut:], src[:, cut:]).then_inc(last_half_loaded, 16)
            for half in range(TILES):
                sp.wait_ge(selected, 1 + half)
                own = slice(TILE_GROUPS * half, TILE_GROUPS * (half + 1))
                sp.dma_start(out[:, own, :], result[:, own, :]).then_inc(out_stored, 16)
            sp.wait_ge(out_stored, 32)

        @block.tensor
        def _(pe):
            def multiply(chunk, start=False, stop=False):
                for t in range(TILES):
                    first = DIM + TILE_ROWS * t
                    mm = nc.tensor.matmul(products[DIM * t:DIM * (t + 1), 0:TILE_ROWS], chunk[:, 0:DIM],
                                          chunk[:, first:first + TILE_ROWS], start=start, stop=stop)
                return mm

            def add_by_row(half, held, streamed, width, stop=False):
                for h in range(TILE_GROUPS):
                    for t in range(TILES):
                        rows = P * (TILE_GROUPS * half + h) + DIM * t
                        mm = nc.tensor.matmul(groups[DIM * t:DIM * (t + 1), half, h, 0:width],
                                              held[:, rows:rows + DIM], streamed, start=False, stop=stop,
                                              skip_group_check=True)
                return mm

            for i, n in enumerate(HEAD_CHUNKS):
                pe.wait_ge(head_loaded[i], 16)
                multiply(head[0:n, i, :], start=(i == 0))
            with pe.Fori(0, ROUNDS) as r:
                for s in range(SLOTS):
                    pe.wait_ge(slot_loaded[s], (r + 1) * 16)
                    for c in range(CHUNKS):
                        mm = multiply(ring[:, s, c, :])
                    mm.then_inc(slot_used[s], 1)
            for i in range(SINGLE, RING_CHUNKS):
                pe.wait_ge(single_loaded[i - SINGLE], 16)
                mm = multiply(ring[:, i // CHUNKS % SLOTS, i % CHUNKS, :], stop=(i == RING_CHUNKS - 1))
            mm.then_inc(products_done, 1)

            pe.wait_ge(identity_step, 1 + TILES)
            pe.wait_ge(products_copied, 1)
            for t in range(TILES):
                lanes = slice(DIM * t, DIM * (t + 1))
                for h in range(TILE_GROUPS):
                    nc.tensor.matmul(groups[:, t, h, 1:], turned_in[lanes, P * h:P * (h + 1)], identity[lanes, :],
                                     is_transpose=True, start=(h == 0), stop=False, skip_group_check=True)
            pe.wait_ge(ones_set, 1)
            for c in range(TAIL - 1):
                if c == TAIL - 5:
                    pe.wait_ge(lanes_summed, 2 + LANE_CHUNKS)
                    for half in range(TILES):
                        add_by_row(half, lane_sum, tail[:, 0, 0:1], 1)
                pe.wait_ge(tail_loaded[c], 16)
                for half in range(TILES):
                    add_by_row(half, tail[:, c, 1 + DIM:], tail[:, c, 0:1 + DIM], 1 + DIM)
            for half, loaded in enumerate([tail_loaded[TAIL - 1], last_half_loaded]):
                pe.wait_ge(loaded, 16)
                add_by_row(half, tail[:, TAIL - 1, 1 + DIM:], tail[:, TAIL - 1, 0:1 + DIM], 1 + DIM,
                           stop=True).then_inc(half_done, 1)

        @block.vector
        def _(dve):
            def add_block(s, adds):
                nc.vector.tensor_tensor(lane_acc[:, :, :], ring[:, s, 0:LANE_CHUNKS, DIM:], lane_acc[:, :, :],
                                        ALU.add).then_inc(block_added, 1)
                dve.wait_ge(block_added, adds)
                dve.sem_inc(slot_used[s], 1)

            nc.vector.memset(lane_acc[:, :, :], 0.0).then_inc(sums_cleared, 1)
            dve.wait_ge(sums_cleared, 1)
            for i, n in enumerate(HEAD_CHUNKS):
                dve.wait_ge(head_loaded[i], 16)
                nc.vector.tensor_tensor(lane_acc[0:n, i, :], head[0:n, i, DIM:], lane_acc[0:n, i, :],
                                        ALU.add).then_inc(head_added, 1)
            dve.wait_ge(head_added, len(HEAD_CHUNKS))
            with dve.Fori(0, ROUNDS) as r:
                for s in range(SLOTS):
                    dve.wait_ge(slot_loaded[s], (r + 1) * 16)
                    add_block(s, r * SLOTS + s + 1)
            for c in range(LANE_CHUNKS):
                dve.wait_ge(single_loaded[c], 16)
            add_block((RING_BLOCKS - 1) % SLOTS, RING_BLOCKS)
            nc.vector.tensor_reduce(lane_total[:, :], lane_acc[:, :, :].rearrange("p c r -> p r c"), AX.X,
                                    ALU.add).then_inc(lanes_summed, 1)
            for c in range(LANE_CHUNKS):
                dve.wait_ge(single_loaded[CHUNKS + c], 16)
                dve.wait_ge(lanes_summed, 1 + c)
                nc.vector.tensor_tensor(lane_total[:, :], ring[:, RING_BLOCKS % SLOTS, c, DIM:], lane_total[:, :],
                                        ALU.add).then_inc(lanes_summed, 1)
            dve.wait_ge(pool_added, RING_BLOCKS)
            dve.wait_ge(lanes_summed, 1 + LANE_CHUNKS)
            nc.vector.tensor_tensor(lane_sum[:, :], pool_acc[:, :], lane_total[:, :],
                                    ALU.add).then_inc(lanes_summed, 1)

            def own(half):
                return slice(TILE_GROUPS * half, TILE_GROUPS * (half + 1))

            def look_at_sums(half):
                dve.wait_ge(half_done, 1 + half)
                nc.vector.tensor_scalar(positive[:, own(half)], groups[:, half, :, 0], 0.0, None,
                                        ALU.is_gt).then_inc(compared, 1)
                nc.vector.reciprocal(inverse[:, own(half)], groups[:, half, :, 0]).then_inc(inverted, 1)

            def select(half):
                dve.wait_ge(compared, 1 + half)
                nc.vector.copy_predicated(result[:, own(half), :],
                                          positive[:, own(half)].unsqueeze(2).broadcast_to([P, TILE_GROUPS, DIM]),
                                          quotient[:, own(half), :]).then_inc(selected, 1)

            look_at_sums(0)
            dve.wait_ge(inverted, 1)
            nc.vector.tensor_tensor(quotient[:, own(0), :], groups[:, 0, :, 1:],
                                    inverse[:, own(0)].unsqueeze(2).broadcast_to([P, TILE_GROUPS, DIM]),
                                    ALU.mult).then_inc(first_half_divided, 1)
            look_at_sums(1)
            dve.wait_ge(result_cleared, 1)
            dve.wait_ge(first_half_divided, 1)
            select(0)
            dve.wait_ge(second_half_divided, TILE_GROUPS)
            select(1)

        @block.scalar
        def _(act):
            act.wait_ge(products_done, 1)
            nc.scalar.copy(turned_in[:, :], products[:, 0:TILE_ROWS]).then_inc(products_copied, 1)
            act.wait_ge(inverted, 2)
            for h in range(TILE_GROUPS):
                g = TILE_GROUPS + h
                nc.scalar.activation(quotient[:, g, :], groups[:, 1, h, 1:], ACT.Copy,
                                     scale=inverse[:, g:g + 1]).then_inc(second_half_divided, 1)

        @block.gpsimd
        def _(pool):
            def add_chunk(s, adds):
                nc.gpsimd.tensor_tensor(pool_acc[:, :], ring[:, s, LANE_CHUNKS, DIM:], pool_acc[:, :],
                                        ALU.add).then_inc(pool_added, 1)
                pool.wait_ge(pool_added, adds)
                pool.sem_inc(slot_used[s], 1)

            nc.gpsimd.memset(pool_acc[:, :], 0.0).then_inc(pool_cleared, 1)
            nc.gpsimd.memset(identity[:, :], 0.0).then_inc(identity_step, 1)
            nc.gpsimd.memset(tail[:, :, 0:1], 1.0).then_inc(ones_set, 1)
            nc.gpsimd.memset(result[:, :, :], 0.0).then_inc(result_cleared, 1)
            for t in range(TILES):
                pool.wait_ge(identity_step, 1 + t)
                nc.gpsimd.affine_select(out=identity[:, :], in_=identity[:, :], compare_op=ALU.not_equal, fill=1.0,
                                        base=-DIM * t, pattern=[[-1, DIM]],
                                        channel_multiplier=1).then_inc(identity_step, 1)
            pool.wait_ge(pool_cleared, 1)
            with pool.Fori(0, ROUNDS) as r:
                for s in range(SLOTS):
                    pool.wait_ge(slot_loaded[s], (r + 1) * 16)
                    add_chunk(s, r * SLOTS + s + 1)
            pool.wait_ge(single_loaded[LANE_CHUNKS], 16)
            add_chunk((RING_BLOCKS - 1) % SLOTS, RING_BLOCKS)


def kernel(r_inputs, L0_rec_embeddings):
    import numpy as np
    import concourse.bacc as bacc
    from concourse.bass_utils import run_bass_kernel_spmd

    packed = np.concatenate([np.asarray(L0_rec_embeddings), np.asarray(r_inputs).T], axis=1)
    nc = bacc.Bacc("TRN2", target_bir_lowering=False, num_devices=1)
    packed_dram = nc.dram_tensor("packed_dram", packed.shape, F32, kind="ExternalInput").ap()
    out_dram = nc.dram_tensor("out_dram", (P, GROUPS, DIM), F32, kind="ExternalOutput").ap()
    weighted_mean_kernel(nc, packed_dram, out_dram)
    ran = run_bass_kernel_spmd(nc, [{"packed_dram": packed}], core_ids=[0])
    return np.ascontiguousarray(ran.results[0]["out_dram"].transpose(1, 0, 2)).reshape(ROWS, DIM)
```
